# Optimizing a Trainium2 kernel written in Bass

```python
import numpy as np
import jax
import jax.numpy as jnp

def _softmax(x, axis=-1):
    return jax.nn.softmax(x, axis=axis)

def _gelu(x):
    return jax.nn.gelu(x, approximate=True)

def _silu(x):
    return jax.nn.silu(x)

def _sigmoid(x):
    return jax.nn.sigmoid(x)

def _layernorm(x, axis=-1, eps=1e-05):
    m = jnp.mean(x, axis=axis, keepdims=True)
    v = jnp.var(x, axis=axis, keepdims=True)
    return (x - m) / jnp.sqrt(v + eps)

def _scatter_add(tgt, idx, src, axis=0):
    return tgt.at[idx].add(src)

def _segment_sum(src, seg, n):
    return jax.ops.segment_sum(src, seg, n)
kernel_name = 'mk_decoder_preln_d1_seqx_r8_ab15ef'

def setup_inputs(seed: int=0):
    np.random.seed(seed)
    _w = jnp.asarray

    def _rec_inputs():
        import jax
        import jax.numpy as jnp
        _rk = jax.random.key(seed)
        x = 7.22e-05 + 1 * jax.random.normal(jax.random.fold_in(_rk, 1), (64, 64, 256), jnp.float32)
        _lenS = 64 - jax.random.randint(jax.random.fold_in(_rk, 7), (64,), 0, max(1, 64 // 4) + 1, jnp.int32)
        _lenS2 = 64 - jax.random.randint(jax.random.fold_in(_rk, 8), (64,), 0, max(1, 64 // 4) + 1, jnp.int32)
        _ctx_512P = jax.random.normal(jax.random.fold_in(_rk, 11), (64, 16, 64), jnp.float32)
        _ctx_512c = jax.random.dirichlet(jax.random.fold_in(_rk, 511), 0.3 * jnp.ones((16,), jnp.float32), (64, 64))
        _ctx_512t = jnp.einsum('bsk,bkd->bsd', _ctx_512c, _ctx_512P)
        _ctx_512t = _ctx_512t * jax.lax.rsqrt(jnp.mean(jnp.square(_ctx_512t)) + 1e-12) * 0.953939
        ctx_512 = -0.000514642 + 1.00011 * (_ctx_512t + 0.3 * jax.random.normal(jax.random.fold_in(_rk, 611), (64, 64, 64), jnp.float32))
        return (x, ctx_512)
    x, ctx_512 = _rec_inputs()

    def _L0_attn_setup():
        import jax, jax.numpy as jnp
        import numpy as np
        B, S, E, H, G = (2, 256, 256, 16, 4)
        D = E // H
        key = jax.random.key(seed)
        ks = jax.random.split(key, 7)
        scale = 1.0 / np.sqrt(E)
        x = jax.random.normal(ks[0], (B, S, E), dtype=jnp.float32)
        Wq = jax.random.normal(ks[1], (H, E, D), dtype=jnp.float32) * scale
        bq = jax.random.normal(ks[2], (H, D), dtype=jnp.float32) * 0.02
        Wk = jax.random.normal(ks[3], (G, E, D), dtype=jnp.float32) * scale
        bk = jax.random.normal(ks[4], (G, D), dtype=jnp.float32) * 0.02
        Wv = jax.random.normal(ks[5], (G, E, D), dtype=jnp.float32) * scale
        bv = jax.random.normal(ks[6], (G, D), dtype=jnp.float32) * 0.02
        return {'x': x, 'Wq': Wq, 'bq': bq, 'Wk': Wk, 'bk': bk, 'Wv': Wv, 'bv': bv}
    _L0_attn_all = _L0_attn_setup()
    _L0_attn_in = {k: v for k, v in _L0_attn_all.items() if k in ('Wq', 'bq', 'Wk', 'bk', 'Wv', 'bv')}
    del _L0_attn_all

    def _L0_xattn_setup():
        import jax, jax.numpy as jnp
        import numpy as np
        import math
        D_MODEL = 256
        N_HEADS = 16
        N_GROUPS = 4
        HEADS_PER_GROUP = N_HEADS // N_GROUPS
        HEAD_DIM = D_MODEL // N_HEADS
        B, S = (2, 256)
        key = jax.random.key(seed)
        k1, k2, k3, k4, k5 = jax.random.split(key, 5)
        q = jax.random.normal(k1, (B, S, D_MODEL), dtype=jnp.float32)
        k = jax.random.normal(k2, (B, S, N_GROUPS * HEAD_DIM), dtype=jnp.float32)
        v = jax.random.normal(k3, (B, S, N_GROUPS * HEAD_DIM), dtype=jnp.float32)
        lim = 1.0 / math.sqrt(D_MODEL)
        Wc = jax.random.uniform(k4, (D_MODEL, D_MODEL), minval=-lim, maxval=lim, dtype=jnp.float32)
        bc = jax.random.uniform(k5, (D_MODEL,), minval=-lim, maxval=lim, dtype=jnp.float32)
        return {'q': q, 'k': k, 'v': v, 'Wc': Wc, 'bc': bc}
    _L0_xattn_all = _L0_xattn_setup()
    _L0_xattn_in = {k: v for k, v in _L0_xattn_all.items() if k in ('Wc', 'bc')}
    del _L0_xattn_all

    def _L0_ffn_setup():
        import jax, jax.numpy as jnp
        import numpy as np
        TOP_K = 6
        N_GROUP = 8
        TOPK_GROUP = 3
        CAPACITY = 96
        RSF = 1.0
        key = jax.random.key(seed)
        ks = jax.random.split(key, 8)
        B, S, H = (1, 512, 256)
        E, M = (64, 176)
        MS = 352
        sc = 0.02
        return {'hidden_states': jax.random.normal(ks[0], (B, S, H), jnp.float32), 'gate_weight': jax.random.normal(ks[1], (E, H), jnp.float32) * sc, 'Wg': jax.random.normal(ks[2], (E, M, H), jnp.float32) * sc, 'Wu': jax.random.normal(ks[3], (E, M, H), jnp.float32) * sc, 'Wd': jax.random.normal(ks[4], (E, H, M), jnp.float32) * sc, 'Sg': jax.random.normal(ks[5], (MS, H), jnp.float32) * sc, 'Su': jax.random.normal(ks[6], (MS, H), jnp.float32) * sc, 'Sd': jax.random.normal(ks[7], (H, MS), jnp.float32) * sc}
    _L0_ffn_all = _L0_ffn_setup()
    _L0_ffn_in = {k: v for k, v in _L0_ffn_all.items() if k in ('gate_weight', 'Wg', 'Wu', 'Wd', 'Sg', 'Su', 'Sd')}
    del _L0_ffn_all
    return {'x': x, 'ctx_512': ctx_512, 'L0_attn_Wq': _L0_attn_in['Wq'], 'L0_attn_bq': _L0_attn_in['bq'], 'L0_attn_Wk': _L0_attn_in['Wk'], 'L0_attn_bk': _L0_attn_in['bk'], 'L0_attn_Wv': _L0_attn_in['Wv'], 'L0_attn_bv': _L0_attn_in['bv'], 'L0_xattn_Wc': _L0_xattn_in['Wc'], 'L0_xattn_bc': _L0_xattn_in['bc'], 'L0_ffn_gate_weight': _L0_ffn_in['gate_weight'], 'L0_ffn_Wg': _L0_ffn_in['Wg'], 'L0_ffn_Wu': _L0_ffn_in['Wu'], 'L0_ffn_Wd': _L0_ffn_in['Wd'], 'L0_ffn_Sg': _L0_ffn_in['Sg'], 'L0_ffn_Su': _L0_ffn_in['Su'], 'L0_ffn_Sd': _L0_ffn_in['Sd']}

def reference(x, ctx_512, L0_attn_Wq, L0_attn_bq, L0_attn_Wk, L0_attn_bk, L0_attn_Wv, L0_attn_bv, L0_xattn_Wc, L0_xattn_bc, L0_ffn_gate_weight, L0_ffn_Wg, L0_ffn_Wu, L0_ffn_Wd, L0_ffn_Sg, L0_ffn_Su, L0_ffn_Sd):
    import jax
    import jax.numpy as jnp

    def _L0_attn_ref(x, Wq, bq, Wk, bk, Wv, bv):
        import jax, jax.numpy as jnp
        import numpy as np
        B, S, E, H, G = (2, 256, 256, 16, 4)
        D = E // H
        h, e, d = Wq.shape
        g = Wk.shape[0]
        per = h // g
        s = x.shape[1]
        q = jnp.einsum('bse,hed->bhsd', x, Wq) + bq[None, :, None, :]
        kg = jnp.einsum('bse,ged->bgsd', x, Wk) + bk[None, :, None, :]
        vg = jnp.einsum('bse,ged->bgsd', x, Wv) + bv[None, :, None, :]
        k = jnp.repeat(kg, per, axis=1)
        v = jnp.repeat(vg, per, axis=1)
        scores = jnp.einsum('bhqd,bhkd->bhqk', q, k) * (1.0 / np.sqrt(d))
        causal = jnp.triu(jnp.ones((s, s), dtype=bool), k=1)
        scores = jnp.where(causal[None, None, :, :], -jnp.inf, scores)
        attn = jax.nn.softmax(scores, axis=-1)
        out = jnp.einsum('bhqk,bhkd->bhqd', attn, v)
        return out.transpose(0, 2, 1, 3).reshape(x.shape[0], s, h * d)

    def _L0_xattn_ref(q, k, v, Wc, bc):
        import jax, jax.numpy as jnp
        import numpy as np
        import math
        D_MODEL = 256
        N_HEADS = 16
        N_GROUPS = 4
        HEADS_PER_GROUP = N_HEADS // N_GROUPS
        HEAD_DIM = D_MODEL // N_HEADS
        B, S = (2, 256)
        b, s, _ = q.shape
        qh = q.reshape(b, s, N_GROUPS, HEADS_PER_GROUP, HEAD_DIM).transpose(0, 2, 3, 1, 4)
        kh = k.reshape(b, s, N_GROUPS, HEAD_DIM).transpose(0, 2, 1, 3)
        vh = v.reshape(b, s, N_GROUPS, HEAD_DIM).transpose(0, 2, 1, 3)
        scale = 1.0 / math.sqrt(HEAD_DIM)
        scores = jnp.einsum('bghsd,bgtd->bghst', qh, kh) * scale
        probs = jax.nn.softmax(scores, axis=-1)
        out = jnp.einsum('bghst,bgtd->bghsd', probs, vh)
        out = out.transpose(0, 3, 1, 2, 4).reshape(b, s, D_MODEL)
        return out @ Wc.T + bc

    def _L0_ffn_ref(hidden_states, gate_weight, Wg, Wu, Wd, Sg, Su, Sd):
        import jax, jax.numpy as jnp
        import numpy as np
        TOP_K = 6
        N_GROUP = 8
        TOPK_GROUP = 3
        CAPACITY = 96
        RSF = 1.0
        B, S, H = hidden_states.shape
        E, M, _ = Wg.shape
        K, NG, TG, C = (TOP_K, N_GROUP, TOPK_GROUP, CAPACITY)
        x = hidden_states.reshape(-1, H)
        T = x.shape[0]
        logits = x.astype(jnp.float32) @ gate_weight.astype(jnp.float32).T
        scores = jax.nn.softmax(logits, axis=-1)
        group_scores = scores.reshape(T, NG, E // NG).max(axis=-1)
        _, gidx = jax.lax.top_k(group_scores, TG)
        gmask = jnp.zeros((T, NG), scores.dtype).at[jnp.arange(T)[:, None], gidx].set(1.0)
        smask = jnp.repeat(gmask, E // NG, axis=1)
        tmp_scores = jnp.where(smask > 0, scores, 0.0)
        topk_w, topk_i = jax.lax.top_k(tmp_scores, K)
        topk_w = topk_w * RSF
        flat = topk_i.reshape(-1)
        oh = jax.nn.one_hot(flat, E, dtype=jnp.int32)
        pos = jnp.sum(jnp.cumsum(oh, axis=0) * oh, axis=-1) - 1
        slot = flat * C + jnp.minimum(pos, C - 1)
        tok = jnp.arange(T * K) // K
        buf = jnp.zeros((E * C, H), x.dtype).at[slot].set(x[tok]).reshape(E, C, H)
        g = jnp.einsum('ech,emh->ecm', buf, Wg)
        u = jnp.einsum('ech,emh->ecm', buf, Wu)
        out = jnp.einsum('ecm,ehm->ech', jax.nn.silu(g) * u, Wd).reshape(E * C, H)
        yk = out[slot].reshape(T, K, H)
        y = jnp.sum(yk * topk_w[..., None].astype(yk.dtype), axis=1)
        shared = jax.nn.silu(x @ Sg.T) * (x @ Su.T) @ Sd.T
        return (y + shared).reshape(B, S, H)
    x = x + _L0_attn_ref(_layernorm(x, axis=-1), L0_attn_Wq, L0_attn_bq, L0_attn_Wk, L0_attn_bk, L0_attn_Wv, L0_attn_bv)
    x = x + _L0_xattn_ref(_layernorm(x, axis=-1), ctx_512, ctx_512, L0_xattn_Wc, L0_xattn_bc)
    x = x + _L0_ffn_ref(_layernorm(x, axis=-1), L0_ffn_gate_weight, L0_ffn_Wg, L0_ffn_Wu, L0_ffn_Wd, L0_ffn_Sg, L0_ffn_Su, L0_ffn_Sd)
    return x

_drawn_inputs = setup_inputs


def setup_inputs(seed=0):
    import zlib

    import numpy as np

    out = dict(_drawn_inputs(seed))
    spreads = {}
    factors = {'L0_attn_bq': 8.0,
     'L0_attn_bk': 8.0,
     'L0_attn_bv': 2.76,
     'L0_ffn_gate_weight': 8.0,
     'L0_ffn_Wg': 8.0,
     'L0_ffn_Wu': 8.0,
     'L0_ffn_Wd': 8.0,
     'L0_ffn_Sg': 3.215,
     'L0_ffn_Su': 3.187,
     'L0_ffn_Sd': 3.19}
    for name, (base, spread) in spreads.items():
        noise = np.random.default_rng([zlib.crc32(name.encode()), seed]).standard_normal(out[name].shape)
        drawn = base * np.exp(spread * noise) if base else spread * noise
        out[name] = jnp.asarray(drawn.astype(out[name].dtype))
    for name, factor in factors.items():
        out[name] = (out[name] * factor).astype(out[name].dtype)
    return out
```

```python
import concourse.bass as bass
from concourse import mybir
from contextlib import ExitStack

F32 = mybir.dt.float32
BF16 = mybir.dt.bfloat16
I32 = mybir.dt.int32
U32 = mybir.dt.uint32
ALU = mybir.AluOpType
ACT = mybir.ActivationFunctionType
AX = mybir.AxisListType

B, S, E = 64, 64, 256
H, G, D = 16, 4, 16
NT = B * S // 128
GT = 4
NG = NT // GT
GB = 2 * GT
TOK = 128 * GT
HH = H // 2
VW = D + 1
SCALE = 0.25
EPS = 1e-5
MASKED = -1e30
NR = 3
NE, M = 64, 176
MH = M // 2
MS = 352
NGRP, TOPG, TOPK = 8, 3, 6
CAP = 96
EB = 8
NOKEY = float(2 ** 20)


def due(value):
    return not isinstance(value, int) or value > 0


def ready(eng, value):
    return value if isinstance(value, int) else eng.to_reg(value)


class Ring:

    def __init__(self, before, body, end, last):
        assert len(body) % NR == 0
        self.lists, self.last = {"before": before, "body": body, "end": end}, last
        self.at = {k: {name: j for j, (name, _) in enumerate(v)} for k, v in self.lists.items()}

    def kind(self, i):
        return "before" if i is None else "end" if isinstance(i, int) and i == self.last else "body"

    def count(self, i, j, who=None):
        def among(uses):
            return sum(w is not None and who in (None, w) for _, w in uses)
        here = among(self.lists[self.kind(i)][:j + 1])
        return here if i is None else among(self.lists["before"]) + i * among(self.lists["body"]) + here

    def use(self, i, name):
        return self.at[self.kind(i)][name]

    def bank(self, i, name):
        j = self.use(i, name)
        return (j if i is None else len(self.lists["before"]) + j) % NR

    def filled(self, i, name):
        return self.count(i, self.use(i, name))

    def emptied(self, i, name):
        j = self.use(i, name) - NR
        if j < 0 and i is None:
            return None, 0
        if j < 0:
            i = before(i)
            j += len(self.lists[self.kind(i)])
        if self.lists[self.kind(i)][j][1] is None:
            j -= NR
        who = self.lists[self.kind(i)][j][1]
        return who, self.count(i, j, who)

    def done(self, i, name):
        j = self.use(i, name)
        who = self.lists[self.kind(i)][j][1]
        return who, self.count(i, j, who)


def first(i):
    return isinstance(i, int) and i == 0


def before(i):
    return None if first(i) else i - 1


def steps(eng, body, apart=1, n=NG):
    for i in range(apart):
        body(i, True)
    with eng.Fori(apart, n - 1) as i:
        body(i, True)
    body(n - 1, False)


def attention_phase(nc, ctx, mem, w, cross):
    p = "x" if cross else "s"

    def sem(name):
        return ctx.enter_context(nc.semaphore(f"{p}_{name}"))

    X, ident, ident_bf, mask, headmask, half_pow = (mem[k] for k in
                                                    ("X", "ident", "ident_bf", "mask", "headmask", "half_pow"))
    xh, xhT, qT, kT, kbd, vT, vbd, ET, E_, mx, mv, st, rstd, rc, att = (
        mem[k] for k in ("xh", "xhT", "qT", "kT", "kbd", "vT", "vbd", "ET", "E", "mx", "mv", "st", "rstd", "rc", "att"))
    ring, Sc, O = mem["ring"], mem["Sc"], mem["O"]

    s_in = sem("inputs")
    s_x0 = sem("x_first")
    s_x = sem("x_rest")
    s_ctx = sem("ctx")
    s_ctx2 = sem("ctx_twice")
    s_st = sem("ln_stats")
    s_mv = sem("ln_meanvar")
    s_ve = sem("ln_vareps")
    s_rs = sem("ln_rstd")
    s_xh = sem("ln_out")
    s_fill = sem("ring_filled")
    s_act = sem("ring_act")
    s_dve = sem("ring_dve")
    s_kbd = sem("kbd")
    s_vps = sem("v_psum")
    s_v = sem("v_ready")
    s_sc = sem("scores")
    s_mx = sem("score_max")
    s_sub = sem("score_shift")
    s_exp = sem("exp")
    s_pv = sem("pv")
    s_rc = sem("recip")
    s_att = sem("att")
    s_res = sem("residual")
    s_rep = sem("repeated")
    s_b = sem("bias_added")
    emptied = {"act": s_act, "dve": s_dve}

    if cross:
        PRO = [("XT0", "act"), ("XT1", "act"), ("K0", "act"), ("K1", "dve")]
        BODY = [("TP00", "act"), ("TP01", "dve"), ("XT0", "act"), ("XT1", "act"),
                ("TP10", "act"), ("TP11", "dve"), ("OT0", "act"), ("K0", "act"), ("K1", "dve"), ("WC0", "dve"),
                ("TP20", "act"), ("TP21", "dve"), ("OT1", "act"), ("WC1", "dve"),
                ("TP30", "act"), ("TP31", "dve"), ("OT2", "act"), ("WC2", "dve"), ("OT3", "act"), ("WC3", "dve"),
                ("none", None)]
    else:
        PRO = [("XT0", "act"), ("XT1", "act"), ("K0", "act"), ("K1", "dve"), ("Q0", "act"), ("Q1", "act"), ("V", "act")]
        BODY = [("TP00", "act"), ("TP01", "dve"), ("XT0", "act"), ("XT1", "act"),
                ("TP10", "act"), ("TP11", "dve"), ("K0", "act"), ("K1", "dve"),
                ("TP20", "act"), ("TP21", "dve"), ("Q0", "act"), ("Q1", "act"),
                ("TP30", "act"), ("TP31", "dve"), ("V", "act")]
    EARLY = ("XT0", "XT1", "K0", "K1", "Q0", "Q1", "V")
    full = Ring(PRO, BODY, [u for u in BODY if u[0] not in EARLY], NG - 1)

    def bank(i, name):
        return ring[full.bank(i, name)]

    def held(i, name):
        who, value = full.emptied(i, name)
        return (emptied[who], value) if who else None

    def filled(i, name):
        return full.filled(i, name)

    def saved(i, name):
        who, value = full.done(i, name)
        return emptied[who], value

    with nc.Block() as block:

        @block.sync
        def _(sp):
            def block_keys(i):
                for c in range(2):
                    sp.wait_ge(*saved(i, f"K{c}"))
                    for h in range(HH):
                        rows = slice(D * h, D * (h + 1))
                        sp.dma_start(kbd[rows, c, :, h, :],
                                     kT[rows, c, :].rearrange("p (b k) -> p b k", k=S)).then_inc(s_kbd, 16)

            if not cross:
                x_rows = w["x"].rearrange("(n p) e -> p n e", p=128)
                sp.dma_start(X[:, 0:GT, :], x_rows[:, 0:GT, :]).then_inc(s_x0, 16)
                sp.dma_start(w["wq_sb"][:], w["wq"].rearrange("(c p) n -> p c n", p=128)).then_inc(s_in, 16)
                sp.dma_start(w["wk_sb"][:], w["wk"].rearrange("(c p) n -> p c n", p=128)).then_inc(s_in, 16)
                sp.dma_start(w["wv_sb"][:], w["wv"].rearrange("(c p) n -> p c n", p=128)).then_inc(s_in, 16)
                sp.dma_start(w["bq_sb"][:], w["bq"]).then_inc(s_in, 16)
                sp.dma_start(w["bv_sb"][:], w["bv"]).then_inc(s_in, 16)
                for g in range(G):
                    for r in range(H // G):
                        at = (g % 2) * 64 + r * D
                        sp.dma_start(w["bk_sb"][at:at + D, g // 2:g // 2 + 1],
                                     w["bk"][g * D:(g + 1) * D, :]).then_inc(s_in, 16)
                for g in range(1, NG):
                    sp.dma_start(X[:, g * GT:(g + 1) * GT, :], x_rows[:, g * GT:(g + 1) * GT, :]).then_inc(s_x, 16)
                block_keys(None)
                block_keys(0)
                with sp.Fori(1, NG - 1) as i:
                    block_keys(i)
            else:
                sp.dma_start(w["wc_sb"][:], w["wc"].rearrange("(c p) n -> p c n", p=128)).then_inc(s_in, 16)
                sp.dma_start(w["bc_sb"][:], w["bc"].partition_broadcast(128)).then_inc(s_in, 16)
                ctx_rows = w["ctx"].rearrange("(g n p) e -> g p n e", p=128, n=GT)
                ctx_keys = w["ctx"].rearrange("(g b k) e -> g k b e", k=S, b=GB)

                def load_ctx(g):
                    sp.dma_start(w["ctxA"][:], ctx_rows[g]).then_inc(s_ctx, 16)

                def load_ctx2(g):
                    sp.dma_start(w["ctx2"][0:64], ctx_keys[g]).then_inc(s_ctx2, 16)
                    sp.dma_start(w["ctx2"][64:128], ctx_keys[g]).then_inc(s_ctx2, 16)

                load_ctx(0)
                load_ctx2(0)
                sp.wait_ge(s_rep, 1)
                load_ctx(1)
                block_keys(None)

                def body(i, more):
                    sp.wait_ge(s_v, 2 * i + 2)
                    load_ctx2(i + 1)
                    sp.wait_ge(s_rep, i + 2)
                    if not isinstance(i, int) or i < NG - 2:
                        load_ctx(i + 2)
                    block_keys(i)

                body(0, True)
                with sp.Fori(1, NG - 2) as i:
                    body(i, True)
                body(NG - 2, True)
                sp.wait_ge(s_v, 2 * NG)
            sp.wait_ge(s_in, (5 + G * (H // G)) * 16 if not cross else 32)

        @block.tensor
        def _(pe):
            def xt(i, g):
                for c in range(2):
                    if held(i, f"XT{c}"):
                        pe.wait_ge(*held(i, f"XT{c}"))
                    out = bank(i, f"XT{c}")
                    for t in range(GT):
                        if c == 0:
                            pe.wait_ge(s_xh, GT * g + t + 1)
                        last = nc.tensor.transpose(out[:, 128 * t:128 * (t + 1)],
                                                   xh[:, t, 128 * c:128 * (c + 1)], ident[:])
                    last.then_inc(s_fill, 1)

            def project(i, name, weight, rows):
                if held(i, name):
                    pe.wait_ge(*held(i, name))
                out = bank(i, name)
                for c in range(2):
                    last = nc.tensor.matmul(out[0:rows, :], weight(c), xhT[:, c, :], start=c == 0, stop=c == 1)
                last.then_inc(s_fill, 1)

            def keys(i, g):
                if cross:
                    pe.wait_ge(s_rep, g + 1)
                    for c in range(2):
                        if held(i, f"K{c}"):
                            pe.wait_ge(*held(i, f"K{c}"))
                        out = bank(i, f"K{c}")
                        for t in range(GT):
                            last = nc.tensor.transpose(out[:, 128 * t:128 * (t + 1)],
                                                       w["ctxR"][:, t, 128 * c:128 * (c + 1)], ident[:])
                        last.then_inc(s_fill, 1)
                else:
                    pe.wait_ge(*saved(i, "XT0"))
                    pe.wait_ge(*saved(i, "XT1"))
                    for c in range(2):
                        project(i, f"K{c}", lambda e, c=c: w["wkr_sb"][:, e, 128 * c:128 * (c + 1)], 128)

            def queries(i):
                for c in range(2):
                    project(i, f"Q{c}", lambda e, c=c: w["wq_sb"][:, e, 128 * c:128 * (c + 1)], 128)

            def scores(i, t):
                n = GT * i + t
                if t == 0:
                    pe.wait_ge(s_kbd, 32 * HH * (i + 1))
                    pe.wait_ge(*saved(before(i), "XT1" if cross else "Q1"))
                    pe.wait_ge(*saved(before(i), "XT0" if cross else "Q0"))
                if due(n - 1):
                    pe.wait_ge(s_sub, n - 1)
                for c in range(2):
                    if not cross:
                        nc.tensor.matmul(Sc[t % 2][:, c, :], ident_bf[:], mask[:], start=True, stop=False)
                    for b in range(2):
                        at = 128 * t + 64 * b
                        last = nc.tensor.matmul(Sc[t % 2][64 * b:64 * (b + 1), c, :], qT[:, c, at:at + 64],
                                                kbd[:, c, 2 * t + b].rearrange("p h k -> p (h k)"),
                                                start=cross, stop=True)
                last.then_inc(s_sc, 1)

            def probs_t(i, t):
                n = GT * i + t
                pe.wait_ge(s_exp, n + 1)
                for c in range(2):
                    if held(i, f"TP{t}{c}"):
                        pe.wait_ge(*held(i, f"TP{t}{c}"))
                    out = bank(i, f"TP{t}{c}")
                    for j in range(4):
                        at = 512 * c + 128 * j
                        last = nc.tensor.transpose(out[:, 128 * j:128 * (j + 1)], E_[:, t % 2, at:at + 128], ident[:])
                    last.then_inc(s_fill, 1)

            def pv(i, t):
                n = GT * i + t
                if t == 0:
                    pe.wait_ge(s_v, 2 * i + 2)
                pe.wait_ge(*saved(i, f"TP{t}0"))
                pe.wait_ge(*saved(i, f"TP{t}1"))
                if due(n):
                    pe.wait_ge(s_att, n)
                for b in range(2):
                    for j in range(H // 2):
                        last = nc.tensor.matmul(
                            O[64 * b:64 * (b + 1), 2 * VW * j:2 * VW * (j + 1)], ET[:, t % 2, j, 64 * b:64 * (b + 1)],
                            vbd[:, 2 * t + b, j // 2].rearrange("p a v -> p (a v)"), start=True, stop=True)
                last.then_inc(s_pv, 1)

            def values_t(i):
                used, (s_saved, count) = ready(pe, GT * i), saved(before(i), "V")
                count = ready(pe, count)
                pe.wait_ge(s_saved, 1)
                pe.wait_ge(s_saved, count)
                if due(used):
                    pe.wait_ge(s_att, used)
                for b in range(GB):
                    last = nc.tensor.transpose(O[:, 64 * b:64 * (b + 1)],
                                               vT[:, b].rearrange("p a k -> p (a k)"), ident[0:64, 0:64])
                last.then_inc(s_vps, 1)

            def out_t(i, t):
                n = GT * i + t
                pe.wait_ge(s_att, n + 1)
                if held(i, f"OT{t}"):
                    pe.wait_ge(*held(i, f"OT{t}"))
                out = bank(i, f"OT{t}")
                for c in range(2):
                    last = nc.tensor.transpose(out[:, 128 * c:128 * (c + 1)],
                                               att[:, t % 2, 128 * c:128 * (c + 1)], ident[:])
                last.then_inc(s_fill, 1)

            def wc(i, t):
                if held(i, f"WC{t}"):
                    pe.wait_ge(*held(i, f"WC{t}"))
                out = bank(i, f"WC{t}")
                pe.wait_ge(*saved(i, f"OT{t}"))
                for c in range(2):
                    last = nc.tensor.matmul(out[:, 0:E], w["oT"][:, t % 2, c, :], w["wc_sb"][:, c, :],
                                            start=c == 0, stop=c == 1)
                last.then_inc(s_fill, 1)

            pe.wait_ge(s_in, (5 + G * (H // G)) * 16 if not cross else 32)
            if cross:
                xt(None, 0)
                keys(None, 0)
            else:
                pe.wait_ge(s_rep, 1)
                xt(None, 0)
                keys(None, 0)
                queries(None)
                project(None, "V", lambda e: w["wv_sb"][:, e, :], 64)

            def body(i, more):
                if not cross:
                    values_t(i)
                scores(i, 0)
                scores(i, 1)
                scores(i, 2)
                probs_t(i, 0)
                scores(i, 3)
                if more:
                    xt(i, i + 1)
                pv(i, 0)
                probs_t(i, 1)
                if cross:
                    out_t(i, 0)
                    if more:
                        keys(i, i + 1)
                elif more:
                    keys(i, i + 1)
                pv(i, 1)
                if cross:
                    wc(i, 0)
                probs_t(i, 2)
                if cross:
                    out_t(i, 1)
                elif more:
                    queries(i)
                pv(i, 2)
                if cross:
                    wc(i, 1)
                probs_t(i, 3)
                if cross:
                    out_t(i, 2)
                elif more:
                    project(i, "V", lambda e: w["wv_sb"][:, e, :], 64)
                pv(i, 3)
                if cross:
                    wc(i, 2)
                    out_t(i, 3)
                    wc(i, 3)

            steps(pe, body)

        @block.scalar
        def _(act):
            def copy(i, name, out, scale=None, bias=None):
                act.wait_ge(s_fill, filled(i, name))
                src = bank(i, name)
                if scale is None:
                    nc.scalar.activation(out, src[0:out.shape[0], 0:TOK], ACT.Identity,
                                         bias=0.0 if bias is None else bias).then_inc(s_act, 1)
                else:
                    nc.scalar.activation(out, src[0:out.shape[0], 0:TOK], ACT.Identity,
                                         bias=0.0 if bias is None else bias, scale=scale).then_inc(s_act, 1)

            def exp(i, t):
                n = GT * i + t
                act.wait_ge(s_sub, n + 1)
                nc.scalar.activation(E_[:, t % 2, :], E_[:, t % 2, :], ACT.Exp).then_inc(s_exp, 1)

            def probs(i, t):
                n = GT * i + t
                if due(n - 1):
                    act.wait_ge(s_pv, n - 1)
                copy(i, f"TP{t}0", ET[:, t % 2, 0:4, :].rearrange("p j q -> p (j q)"))

            def xt(i):
                for c in range(2):
                    if cross:
                        copy(i, f"XT{c}", qT[:, c, :], scale=SCALE)
                    else:
                        copy(i, f"XT{c}", xhT[:, c, :])

            def k0(i):
                if cross:
                    copy(i, "K0", kT[:, 0, :])
                else:
                    copy(i, "K0", kT[:, 0, :], bias=w["bk_sb"][:, 0:1])

            def q(i):
                for c in range(2):
                    copy(i, f"Q{c}", qT[:, c, :], scale=SCALE, bias=w["bqs_sb"][:, c:c + 1])

            def v(i):
                act.wait_ge(s_fill, filled(i, "V"))
                src = bank(i, "V")[0:64, :].rearrange("p (b k) -> p b k", k=S)
                nc.scalar.activation(vT[:], src.unsqueeze(2).to_broadcast([64, GB, 2, S]), ACT.Identity,
                                     bias=w["bv_sb"][:]).then_inc(s_act, 1)

            def ot(i, t):
                act.wait_ge(s_fill, filled(i, f"OT{t}"))
                src = bank(i, f"OT{t}")
                nc.scalar.copy(w["oT"][:, t % 2].rearrange("p c q -> p (c q)"), src[:, 0:E]).then_inc(s_act, 1)

            def values(i):
                if cross:
                    act.wait_ge(s_ctx2, 32 * (i + 1))
                else:
                    act.wait_ge(s_vps, i + 1)
                if due(GT * i):
                    act.wait_ge(s_pv, GT * i)
                for h in range(2):
                    rows = slice(64 * h, 64 * (h + 1))
                    src = w["ctx2"][rows].rearrange("p b (g d) -> p b g d", d=D) if cross else \
                        O[rows, :].rearrange("p (b g d) -> p b g d", g=G, d=D)
                    nc.scalar.copy(vbd[rows, :, :, h, 0:D], src).then_inc(s_v, 1)

            act.wait_ge(s_in, (5 + G * (H // G)) * 16 if not cross else 32)
            if not cross:
                nc.scalar.mul(w["bqs_sb"][:], w["bq_sb"][:], SCALE).then_inc(s_b, 1)
            xt(None)
            k0(None)
            if not cross:
                act.wait_ge(s_b, 1)
                q(None)
                v(None)

            def body(i, more):
                values(i)
                exp(i, 0)
                exp(i, 1)
                probs(i, 0)
                exp(i, 2)
                if more:
                    xt(i)
                exp(i, 3)
                probs(i, 1)
                if cross:
                    ot(i, 0)
                if more:
                    k0(i)
                probs(i, 2)
                if cross:
                    ot(i, 1)
                elif more:
                    q(i)
                probs(i, 3)
                if cross:
                    ot(i, 2)
                    ot(i, 3)
                elif more:
                    v(i)

            steps(act, body)

        @block.vector
        def _(dve):
            def stats(g):
                for t in range(GT):
                    nc.vector.bn_stats(st[:, t, :], X[:, GT * g + t, :]).then_inc(s_st, 1)

            def meanvar(g):
                for t in range(GT):
                    count = ready(dve, GT * g + t + 1)
                    dve.wait_ge(s_st, 1)
                    dve.wait_ge(s_st, count)
                    nc.vector.bn_aggr(mv[:, t, :], st[:, t, :]).then_inc(s_mv, 1)

            def normalize(g):
                dve.wait_ge(s_rs, g + 1)
                for t in range(GT):
                    nc.vector.tensor_scalar(xh[:, t, :], X[:, GT * g + t, :], mv[:, t, 0:1], rstd[:, t:t + 1],
                                            ALU.subtract, ALU.mult).then_inc(s_xh, 1)

            def shift(i, t):
                n = GT * i + t
                dve.wait_ge(s_sc, n + 1)
                sc = Sc[t % 2][:, :, :].rearrange("p c (h k) -> p (c h) k", k=S)
                nc.vector.reduce_max(mx[:, t % 2, :], sc, AX.X).then_inc(s_mx, 1)
                dve.wait_ge(s_mx, n + 1)
                if t >= 2:
                    dve.wait_ge(s_fill, filled(i, f"TP{t - 2}1"))
                else:
                    if not first(i):
                        dve.wait_ge(s_fill, filled(i - 1, f"TP{t + 2}1"))
                nc.vector.tensor_tensor(E_[:, t % 2, :].rearrange("p (h k) -> p h k", k=S), sc,
                                        mx[:, t % 2, :].unsqueeze(2).to_broadcast([128, H, S]),
                                        ALU.subtract).then_inc(s_sub, 1)

            def probs(i, t):
                n = GT * i + t
                dve.wait_ge(s_fill, filled(i, f"TP{t}1"))
                src = bank(i, f"TP{t}1")
                if due(n - 1):
                    dve.wait_ge(s_pv, n - 1)
                nc.vector.tensor_copy(ET[:, t % 2, 4:8, :].rearrange("p j q -> p (j q)"), src[:]).then_inc(s_dve, 1)

            def k1(i):
                dve.wait_ge(s_fill, filled(i, "K1"))
                src = bank(i, "K1")
                if cross:
                    nc.vector.tensor_copy(kT[:, 1, :], src[:]).then_inc(s_dve, 1)
                else:
                    nc.vector.tensor_scalar(kT[:, 1, :], src[:], w["bk_sb"][:, 1:2], None, ALU.add).then_inc(s_dve, 1)

            def output(i, t):
                n = GT * i + t
                dve.wait_ge(s_pv, n + 1)
                o = O[:, 0:H * VW].rearrange("p (h v) -> p h v", v=VW)
                nc.vector.reciprocal(rc[:, t % 2, :], o[:, :, D]).then_inc(s_rc, 1)
                dve.wait_ge(s_rc, n + 1)
                if cross:
                    if t >= 2:
                        dve.wait_ge(s_fill, filled(i, f"OT{t - 2}"))
                    elif not first(i):
                        dve.wait_ge(s_fill, filled(i - 1, f"OT{t + 2}"))
                else:
                    if due(n - 1):
                        dve.wait_ge(s_res, n - 1)
                nc.vector.tensor_tensor(att[:, t % 2, :].rearrange("p (h d) -> p h d", d=D), o[:, :, 0:D],
                                        rc[:, t % 2, :].unsqueeze(2).to_broadcast([128, H, D]),
                                        ALU.mult).then_inc(s_att, 1)

            def wc(i, t):
                n = GT * i + t
                dve.wait_ge(s_fill, filled(i, f"WC{t}"))
                src = bank(i, f"WC{t}")
                if t == 0:
                    dve.wait_ge(s_b, i + 1)
                nc.vector.tensor_tensor(X[:, GT * i + t, :], src[:, 0:E], X[:, GT * i + t, :], ALU.add).then_inc(s_dve, 1)

            if not cross:
                dve.wait_ge(s_x0, 16)
            stats(0)
            meanvar(0)
            normalize(0)
            dve.wait_ge(s_in, (5 + G * (H // G)) * 16 if not cross else 32)
            k1(None)
            if not cross:
                dve.wait_ge(s_x, 16 * (NG - 1))

            def body(i, more):
                shift(i, 0)
                if more:
                    stats(i + 1)
                shift(i, 1)
                if more:
                    meanvar(i + 1)
                shift(i, 2)
                if more:
                    dve.wait_ge(s_fill, filled(before(i), "XT1"))
                    normalize(i + 1)
                probs(i, 0)
                shift(i, 3)
                output(i, 0)
                probs(i, 1)
                if more:
                    k1(i)
                output(i, 1)
                if cross:
                    wc(i, 0)
                probs(i, 2)
                output(i, 2)
                if cross:
                    wc(i, 1)
                probs(i, 3)
                output(i, 3)
                if cross:
                    wc(i, 2)
                    wc(i, 3)

            steps(dve, body)

        @block.gpsimd
        def _(pool):
            def deviation(g):
                count = ready(pool, GT * (g + 1))
                pool.wait_ge(s_mv, 1)
                pool.wait_ge(s_mv, count)
                nc.gpsimd.tensor_scalar(rstd[:], mv[:, :, 1], EPS, None, ALU.add).then_inc(s_ve, 1)
                pool.wait_ge(s_ve, g + 1)
                nc.gpsimd.tensor_tensor(rstd[:], rstd[:], half_pow[:, 0:GT], ALU.pow).then_inc(s_rs, 1)

            def residual(i, t):
                n = GT * i + t
                pool.wait_ge(s_att, n + 1)
                nc.gpsimd.tensor_tensor(X[:, GT * i + t, :], X[:, GT * i + t, :], att[:, t % 2, :],
                                        ALU.add).then_inc(s_res, 1)

            def bias(i):
                pool.wait_ge(s_xh, GT * (i + 1))
                nc.gpsimd.tensor_tensor(X[:, bass.ds(GT * i, GT), :], X[:, bass.ds(GT * i, GT), :],
                                        w["bc_sb"][:].unsqueeze(1).to_broadcast([128, GT, E]),
                                        ALU.add).then_inc(s_b, 1)

            def context(g):
                count = ready(pool, 16 * (g + 1))
                used = None if first(g) else ready(pool, filled(before(g - 1), "K1"))
                pool.wait_ge(s_ctx, 1)
                pool.wait_ge(s_ctx, count)
                if not first(g):
                    pool.wait_ge(s_fill, used)
                nc.gpsimd.tensor_copy(
                    w["ctxR"][:].rearrange("p t (g r d) -> p (t g) r d", r=H // G, d=D),
                    w["ctxA"][:].rearrange("p t (g d) -> p (t g) d", d=D).unsqueeze(2).to_broadcast(
                        [128, GT * G, H // G, D])).then_inc(s_rep, 1)

            deviation(0)
            if cross:
                pool.wait_ge(s_in, 32)
                context(0)
            else:
                pool.wait_ge(s_in, (5 + G * (H // G)) * 16)
                for c in range(2):
                    last = nc.gpsimd.tensor_copy(
                        w["wkr_sb"][:, c].rearrange("p (g r d) -> p g r d", r=H // G, d=D),
                        w["wk_sb"][:, c].rearrange("p (g d) -> p g d", d=D).unsqueeze(2).to_broadcast(
                            [128, G, H // G, D]))
                last.then_inc(s_rep, 1)

            def body(i, more):
                if cross:
                    bias(i)
                if more:
                    deviation(i + 1)
                    if cross:
                        context(i + 1)
                if not cross:
                    residual(i, 0)
                if not cross:
                    for t in range(1, GT):
                        residual(i, t)

            steps(pool, body)


def routing_phase(nc, ctx, mem, w):
    def sem(name):
        return ctx.enter_context(nc.semaphore(f"r_{name}"))

    X, ident, half_pow, xnT, WK = (mem[k] for k in ("X", "ident", "half_pow", "xnT", "WK"))
    xn, mv, st, rstd, gate, logT, lg, m4, r4, sc, gs, g8, gi, eqg, gm, tmp, t8, ti, eqe, wa, iota, desc = (
        mem[k] for k in ("xn", "mv", "st", "rstd", "gate", "logT", "lg", "m4", "r4", "sc", "gs", "g8", "gi",
                         "eqg", "gm", "tmp", "t8", "ti", "eqe", "wa", "iota", "desc"))
    P = mem["banks"]
    XP, LP, TP, WP = P[0:2], P[2], P[3], P[4]

    s_in = sem("gate")
    s_st = sem("ln_stats")
    s_mv = sem("ln_meanvar")
    s_ve = sem("ln_vareps")
    s_rs = sem("ln_rstd")
    s_xn = sem("ln_out")
    s_row = sem("rows_stored")
    s_wst = sem("weights_stored")
    s_xt = sem("xt_psum")
    s_xe = sem("xt_saved")
    s_lp = sem("logits_t")
    s_le = sem("logits_t_saved")
    s_lt = sem("logits")
    s_m4 = sem("logit_max")
    s_lg = sem("logit_shift")
    s_ex = sem("logit_exp")
    s_sm = sem("softmax_step")
    s_g8 = sem("groups_sorted")
    s_gi = sem("groups_index")
    s_gm = sem("group_mask")
    s_t8 = sem("experts_sorted")
    s_ti = sem("experts_index")
    s_eq = sem("experts_equal")
    s_wa = sem("weights")
    s_wt = sem("weights_t")
    s_ws = sem("weights_t_saved")
    s_key = sem("keys")

    rows = w["rows"][0:NT * 128, :].rearrange("(g t p) e -> g p t e", p=128, t=GT)

    with nc.Block() as block:
        @block.sync
        def _(sp):
            def body(i, more):
                sp.wait_ge(s_xn, GT * (i + 1))
                sp.dma_start(rows[i, :, :, 0:E], xn[:]).then_inc(s_row, 16)
                sp.wait_ge(s_wa, i + 1)
                sp.dma_start(rows[i, :, :, E:E + NE], wa[:, :, 0:NE]).then_inc(s_wst, 16)

            steps(sp, body)
            sp.wait_ge(s_row, 16 * NG)
            sp.wait_ge(s_wst, 16 * NG)

        @block.tensor
        def _(pe):
            def logits(g):
                if due(2 * g):
                    pe.wait_ge(s_xe, 2 * g)
                for c in range(2):
                    for t in range(GT):
                        if c == 0:
                            pe.wait_ge(s_xn, GT * g + t + 1)
                        last = nc.tensor.transpose(XP[c][:, 128 * t:128 * (t + 1)],
                                                   xn[:, t, 128 * c:128 * (c + 1)], ident[:])
                    last.then_inc(s_xt, 1)
                pe.wait_ge(s_xe, 2 * (g + 1))
                if due(g):
                    pe.wait_ge(s_le, g)
                for c in range(2):
                    last = nc.tensor.matmul(LP[0:NE, :], gate[:, c, :], xnT[:, c, bass.ds(TOK * g, TOK)],
                                            start=c == 0, stop=c == 1)
                last.then_inc(s_lp, 1)
                saved, used = ready(pe, g + 1), ready(pe, g)
                pe.wait_ge(s_le, 1)
                pe.wait_ge(s_le, saved)
                if due(used):
                    pe.wait_ge(s_lg, used)
                for t in range(GT):
                    last = nc.tensor.transpose(TP[:, NE * t:NE * (t + 1)], logT[:, 128 * t:128 * (t + 1)],
                                               ident[0:NE, 0:NE])
                last.then_inc(s_lt, 1)

            def weights_t(g):
                pe.wait_ge(s_wa, g + 1)
                if due(g):
                    pe.wait_ge(s_ws, g)
                if due(g):
                    pe.wait_ge(s_key, g)
                for t in range(GT):
                    last = nc.tensor.transpose(WP[:, 128 * t:128 * (t + 1)], wa[:, t, :], ident[:])
                last.then_inc(s_wt, 1)

            logits(0)

            def body(i, more):
                if more:
                    logits(i + 1)
                weights_t(i)

            steps(pe, body)

        @block.scalar
        def _(act):
            def save(g):
                for c in range(2):
                    act.wait_ge(s_xt, 2 * g + c + 1)
                    nc.scalar.copy(xnT[:, c, bass.ds(TOK * g, TOK)], XP[c][:]).then_inc(s_xe, 1)
                act.wait_ge(s_lp, g + 1)
                nc.scalar.copy(logT[:], LP[0:NE, :]).then_inc(s_le, 1)

            save(0)

            def body(i, more):
                act.wait_ge(s_lg, i + 1)
                nc.scalar.activation(lg[:], lg[:], ACT.Exp).then_inc(s_ex, 1)
                if more:
                    save(i + 1)
                act.wait_ge(s_wt, i + 1)
                nc.scalar.copy(WK[0:NE, bass.ds(TOK * i, TOK)], WP[0:NE, :]).then_inc(s_ws, 1)

            steps(act, body)

        @block.vector
        def _(dve):
            def meanvar(g):
                for t in range(GT):
                    nc.vector.bn_stats(st[:, t, :], X[:, GT * g + t, :]).then_inc(s_st, 1)
                for t in range(GT):
                    count = ready(dve, GT * g + t + 1)
                    dve.wait_ge(s_st, 1)
                    dve.wait_ge(s_st, count)
                    nc.vector.bn_aggr(mv[:, t, :], st[:, t, :]).then_inc(s_mv, 1)

            def normalize(g):
                dve.wait_ge(s_rs, g + 1)
                if due(2 * g):
                    dve.wait_ge(s_xt, 2 * g)
                if due(16 * g):
                    dve.wait_ge(s_row, 16 * g)
                for t in range(GT):
                    nc.vector.tensor_scalar(xn[:, t, :], X[:, GT * g + t, :], mv[:, t, 0:1], rstd[:, t:t + 1],
                                            ALU.subtract, ALU.mult).then_inc(s_xn, 1)

            meanvar(0)
            normalize(0)

            def body(i, more):
                if more:
                    meanvar(i + 1)
                dve.wait_ge(s_lt, i + 1)
                lt = TP[:, 0:GT * NE].rearrange("p (t e) -> p t e", e=NE)
                nc.vector.reduce_max(m4[:], lt, AX.X).then_inc(s_m4, 1)
                dve.wait_ge(s_m4, i + 1)
                nc.vector.tensor_tensor(lg[:], lt, m4[:].unsqueeze(2).to_broadcast([128, GT, NE]),
                                        ALU.subtract).then_inc(s_lg, 1)
                if more:
                    normalize(i + 1)
                dve.wait_ge(s_ex, i + 1)
                nc.vector.reduce_sum(r4[:], lg[:], AX.X).then_inc(s_sm, 1)
                dve.wait_ge(s_sm, 4 * i + 1)
                nc.vector.reciprocal(r4[:], r4[:]).then_inc(s_sm, 1)
                dve.wait_ge(s_sm, 4 * i + 2)
                nc.vector.tensor_tensor(sc[:], lg[:], r4[:].unsqueeze(2).to_broadcast([128, GT, NE]),
                                        ALU.mult).then_inc(s_sm, 1)
                dve.wait_ge(s_sm, 4 * i + 3)
                nc.vector.reduce_max(gs[:], sc[:].rearrange("p t (g e) -> p (t g) e", e=NE // NGRP),
                                     AX.X).then_inc(s_sm, 1)
                count = ready(dve, 4 * i + 4)
                dve.wait_ge(s_sm, 1)
                dve.wait_ge(s_sm, count)
                for t in range(GT):
                    nc.vector.max(g8[:, t, :], gs[:, NGRP * t:NGRP * (t + 1)]).then_inc(s_g8, 1)
                for t in range(GT):
                    count = ready(dve, GT * i + t + 1)
                    dve.wait_ge(s_g8, 1)
                    dve.wait_ge(s_g8, count)
                    nc.vector.max_index(gi[:, t, :], g8[:, t, :], gs[:, NGRP * t:NGRP * (t + 1)]).then_inc(s_gi, 1)
                dve.wait_ge(s_gi, GT * (i + 1))
                nc.vector.tensor_tensor(
                    eqg[:], iota[:, 0:NGRP].unsqueeze(1).unsqueeze(3).to_broadcast([128, GT, NGRP, TOPG]),
                    gi[:, :, 0:TOPG].unsqueeze(2).to_broadcast([128, GT, NGRP, TOPG]), ALU.is_equal).then_inc(s_gm, 1)
                dve.wait_ge(s_gm, 3 * i + 1)
                nc.vector.reduce_sum(gm[:], eqg[:].rearrange("p t g j -> p (t g) j"), AX.X).then_inc(s_gm, 1)
                dve.wait_ge(s_gm, 3 * i + 2)
                nc.vector.tensor_tensor(tmp[:].rearrange("p t (g e) -> p (t g) e", e=NE // NGRP),
                                        sc[:].rearrange("p t (g e) -> p (t g) e", e=NE // NGRP),
                                        gm[:].unsqueeze(2).to_broadcast([128, GT * NGRP, NE // NGRP]),
                                        ALU.mult).then_inc(s_gm, 1)
                count = ready(dve, 3 * i + 3)
                dve.wait_ge(s_gm, 1)
                dve.wait_ge(s_gm, count)
                for t in range(GT):
                    nc.vector.max(t8[:, t, :], tmp[:, t, :]).then_inc(s_t8, 1)
                for t in range(GT):
                    count = ready(dve, GT * i + t + 1)
                    dve.wait_ge(s_t8, 1)
                    dve.wait_ge(s_t8, count)
                    nc.vector.max_index(ti[:, t, :], t8[:, t, :], tmp[:, t, :]).then_inc(s_ti, 1)
                if due(i):
                    dve.wait_ge(s_wt, i)
                if due(16 * i):
                    dve.wait_ge(s_wst, 16 * i)
                for t in range(GT):
                    dve.wait_ge(s_ti, GT * i + t + 1)
                    nc.vector.tensor_tensor(eqe[:, t % 2], iota[:].unsqueeze(2).to_broadcast([128, NE, TOPK]),
                                            ti[:, t, 0:TOPK].unsqueeze(1).to_broadcast([128, NE, TOPK]),
                                            ALU.is_equal).then_inc(s_eq, 1)
                    dve.wait_ge(s_eq, 2 * (GT * i + t) + 1)
                    nc.vector.reduce_sum(wa[:, t, NE:2 * NE], eqe[:, t % 2], AX.X).then_inc(s_eq, 1)
                dve.wait_ge(s_eq, 2 * GT * (i + 1))
                nc.vector.tensor_tensor(wa[:, :, 0:NE], tmp[:], wa[:, :, NE:2 * NE], ALU.mult).then_inc(s_wa, 1)
                dve.wait_ge(s_wt, i + 1)
                nc.vector.tensor_tensor(WK[NE:128, bass.ds(TOK * i, TOK)], WP[NE:128, :],
                                        desc[NE:128, bass.ds(TOK * i, TOK)], ALU.mult).then_inc(s_key, 1)

            steps(dve, body)

        @block.gpsimd
        def _(pool):
            def deviation(g):
                count, used = ready(pool, GT * (g + 1)), ready(pool, GT * g)
                pool.wait_ge(s_mv, 1)
                pool.wait_ge(s_mv, count)
                if due(used):
                    pool.wait_ge(s_xn, used)
                nc.gpsimd.tensor_scalar(rstd[:], mv[:, :, 1], EPS, None, ALU.add).then_inc(s_ve, 1)
                pool.wait_ge(s_ve, g + 1)
                nc.gpsimd.tensor_tensor(rstd[:], rstd[:], half_pow[:, 0:GT], ALU.pow).then_inc(s_rs, 1)

            deviation(0)

            def body(i, more):
                if more:
                    deviation(i + 1)

            steps(pool, body)


def shared_phase(nc, ctx, mem, w):
    def sem(name):
        return ctx.enter_context(nc.semaphore(f"h_{name}"))

    X, ident, xnT, WK, kw, top, tokf, slot, mark, lastk, sg, su, hT, sh, tokens = (
        mem[k] for k in ("X", "ident", "xnT", "WK", "kw", "top", "tokf", "slot", "mark", "lastk", "sg", "su", "hT",
                         "sh", "tokens"))
    P = mem["banks"]
    key = WK[NE:128, :]
    sgu, sd = w["sgu_sb"], w["sd_sb"]
    MC = [(0, 128), (128, 128), (256, MS - 256)]

    s_up = sem("up")
    s_sil = sem("silu")
    s_hid = sem("hidden")
    s_dn = sem("down")
    s_sh = sem("down_saved")
    s_add = sem("added")
    s_top = sem("top")
    s_cut = sem("cut")
    s_lk = sem("last_key")
    s_tok = sem("token_step")
    s_tt = sem("tokens_t")
    s_over = sem("over")

    with nc.Block() as block:
        @block.tensor
        def _(pe):
            def up(i):
                for c, (m0, m) in enumerate(MC):
                    for k in range(2):
                        u = 2 * c + k
                        if not first(i):
                            pe.wait_ge(s_sil, 6 * (i - 1) + u + 1)
                        out = P[u]
                        for e in range(2):
                            last = nc.tensor.matmul(out[0:m, :], sgu[:, e, k * MS + m0:k * MS + m0 + m],
                                                    xnT[:, e, bass.ds(TOK * i, TOK)], start=e == 0, stop=e == 1)
                        last.then_inc(s_up, 1)

            def down(i):
                for b in range(2):
                    if due(2 * i + b - 1):
                        pe.wait_ge(s_sh, 2 * i + b - 1)
                    pe.wait_ge(s_hid, 3 * (i + 1))
                    for t in (2 * b, 2 * b + 1):
                        for c, (m0, m) in enumerate(MC):
                            last = nc.tensor.matmul(P[6 + b][:, E * (t % 2):E * (t % 2 + 1)],
                                                    hT[0:m, c, 128 * t:128 * (t + 1)], sd[0:m, c, :],
                                                    start=c == 0, stop=c == 2)
                    last.then_inc(s_dn, 1)

            pe.wait_ge(w["s_moe_in"], w["n_moe_in"])
            up(0)

            def body(i, more):
                if more:
                    up(i + 1)
                down(i)

            steps(pe, body)
            pe.wait_ge(s_tok, 7)
            nc.tensor.transpose(P[0][0:CAP, 0:NE], tokf[NE:128, :], ident[NE:128, NE:128]).then_inc(s_tt, 1)

        @block.scalar
        def _(act):
            def body(i, more):
                for c, (m0, m) in enumerate(MC):
                    act.wait_ge(s_up, 6 * i + 2 * c + 1)
                    if not first(i):
                        act.wait_ge(s_hid, 3 * (i - 1) + c + 1)
                    nc.scalar.activation(sg[0:m, c, :], P[2 * c][0:m, :],
                                         ACT.Silu).then_inc(s_sil, 1)
                    act.wait_ge(s_up, 6 * i + 2 * c + 2)
                    nc.scalar.copy(su[0:m, c, :],
                                   P[2 * c + 1][0:m, :]).then_inc(s_sil, 1)
                if not first(i):
                    save(i - 1)

            def save(i):
                for b in range(2):
                    act.wait_ge(s_dn, 2 * i + b + 1)
                    if due(i):
                        act.wait_ge(s_add, i)
                    nc.scalar.copy(sh[:, 2 * b:2 * b + 2, :].rearrange("p t e -> p (t e)"),
                                   P[6 + b][:]).then_inc(s_sh, 1)

            steps(act, body, apart=2)
            save(NG - 1)

        @block.gpsimd
        def _(pool):
            def body(i, more):
                for c, (m0, m) in enumerate(MC):
                    pool.wait_ge(s_sil, 6 * i + 2 * c + 2)
                    if due(2 * i):
                        pool.wait_ge(s_dn, 2 * i)
                    nc.gpsimd.tensor_tensor(hT[0:m, c, :], sg[0:m, c, :], su[0:m, c, :], ALU.mult).then_inc(s_hid, 1)
                if not first(i):
                    add(i - 1)

            def add(i):
                pool.wait_ge(s_sh, 2 * (i + 1))
                nc.gpsimd.tensor_tensor(X[:, bass.ds(GT * i, GT), :], X[:, bass.ds(GT * i, GT), :], sh[:],
                                        ALU.add).then_inc(s_add, 1)

            steps(pool, body)
            add(NG - 1)

        @block.vector
        def _(dve):
            for r in range(CAP // 8):
                src = key if r == 0 else kw[NE:128, :]
                if due(r):
                    dve.wait_ge(s_cut, r)
                nc.vector.max(top[NE:128, 8 * r:8 * r + 8], src).then_inc(s_top, 1)
                dve.wait_ge(s_top, r + 1)
                nc.vector.match_replace(kw[NE:128, :], top[NE:128, 8 * r:8 * r + 8], src, 0.0).then_inc(s_cut, 1)
            dve.wait_ge(s_cut, CAP // 8)
            nc.vector.tensor_scalar(kw[NE:128, :], key, 0.0, NOKEY, ALU.is_equal, ALU.mult).then_inc(s_tok, 1)
            dve.wait_ge(s_tok, 1)
            nc.vector.tensor_tensor(kw[NE:128, :], kw[NE:128, :], key, ALU.add).then_inc(s_tok, 1)
            dve.wait_ge(s_tok, 2)
            nc.vector.tensor_reduce(lastk[NE:128, 0:1], kw[NE:128, :], AX.X, ALU.min).then_inc(s_tok, 1)
            dve.wait_ge(s_tok, 3)
            nc.vector.tensor_scalar(lastk[NE:128, 1:2], lastk[NE:128, 0:1], float(NT * 128),
                                    -(NOKEY + CAP - 1), ALU.is_gt, ALU.mult).then_inc(s_tok, 1)
            nc.vector.tensor_scalar(mark[NE:128, :], top[NE:128, :], 0.0, None, ALU.is_equal).then_inc(s_tok, 1)
            dve.wait_ge(s_tok, 5)
            nc.vector.tensor_tensor(mark[NE:128, :], mark[NE:128, :], slot[NE:128, :], ALU.mult).then_inc(s_tok, 1)
            dve.wait_ge(s_tok, 6)
            nc.vector.scalar_tensor_tensor(out=mark[NE:128, :], in0=top[NE:128, :], scalar=-1.0,
                                           in1=mark[NE:128, :], op0=ALU.mult, op1=ALU.add).then_inc(s_cut, 1)
            nc.vector.tensor_tensor(lastk[NE:128, 2:3], lastk[NE:128, 0:1], lastk[NE:128, 1:2],
                                    ALU.add).then_inc(s_cut, 1)
            dve.wait_ge(s_cut, CAP // 8 + 2)
            nc.vector.tensor_scalar(tokf[NE:128, 0:CAP - 1], mark[NE:128, 0:CAP - 1], float(NT * 128), None, ALU.add)
            nc.vector.tensor_scalar(tokf[NE:128, CAP - 1:CAP], lastk[NE:128, 2:3], -1.0, float(NT * 128),
                                    ALU.mult, ALU.add).then_inc(s_tok, 1)
            dve.wait_ge(s_tt, 1)
            nc.vector.tensor_copy(tokens[:], P[0][0:CAP, 0:NE])
            nc.vector.tensor_scalar(kw[0:NE, :], key, top[NE:128, CAP - 2:CAP - 1], None, ALU.is_lt).then_inc(s_over, 1)
            dve.wait_ge(s_over, 1)
            nc.vector.tensor_tensor(WK[0:NE, :], WK[0:NE, :], kw[0:NE, :], ALU.mult)


def experts_phase(nc, ctx, mem, w):
    def sem(name):
        return ctx.enter_context(nc.semaphore(f"e_{name}"))

    ident, tokens, gidx, sidx, xg, xT, sil, hid, outs, wcol, own, lastone = (
        mem[k] for k in ("ident", "tokens", "gidx", "sidx", "xg", "xT", "sil", "hid", "outs", "wcol", "own", "lastone"))
    wgu, wd = w["wgu_sb"], w["wd_sb"]
    P = mem["banks"]
    XP, GP, DP = P[0:2], P[2:4], P[4:6]
    s_w = w["s_w"]

    s_gi = sem("gather_list")
    s_si = sem("scatter_list")
    s_g = [sem(f"gathered{j}") for j in range(EB)]
    s_x = sem("rows_t")
    s_xe = sem("rows_t_saved")
    s_wc = sem("slot_weights")
    s_gu = sem("gate_up")
    s_sil = sem("silu")
    s_h = sem("hidden")
    s_d = sem("down")
    s_o = sem("weighted")
    s_s = [sem(f"added{k}") for k in range(2)]
    s_l = [sem(f"last_stored{j}") for j in range(EB)]

    NB = NE // EB

    with nc.Block() as block:
        @block.sync
        def _(sp):
            def body(i, more):
                for j in range(EB):
                    e = EB * i + j
                    if more:
                        sp.wait_ge(s_gu, e + 1)
                        sp.dma_start(wgu[:, j, :], w["wgu"][e + EB]).then_inc(s_w[j], 16)
                        sp.wait_ge(s_d, e + 1)
                        sp.dma_start(wd[:, j, :], w["wd"][e + EB]).then_inc(s_w[j], 16)

            steps(sp, body, n=NB)

        @block.tensor
        def _(pe):
            def rows_t(i, j):
                e = EB * i + j
                pe.wait_ge(s_g[j], 16 * (i + 1))
                if due(e - 1):
                    pe.wait_ge(s_xe, e - 1)
                for c in range(2):
                    last = nc.tensor.transpose(XP[j % 2][:, CAP * c:CAP * (c + 1)],
                                               xg[:, j, 128 * c:128 * (c + 1)], ident[0:CAP, 0:CAP])
                last.then_inc(s_x, 1)

            def gate_up(i, j):
                e = EB * i + j
                pe.wait_ge(s_w[j], 32 * (i + 1))
                pe.wait_ge(s_xe, e + 1)
                if due(e - 1):
                    pe.wait_ge(s_h, e - 1)
                for u in range(4):
                    for c in range(2):
                        last = nc.tensor.matmul(GP[j % 2][0:MH, CAP * u:CAP * (u + 1)],
                                                wgu[:, j, 4 * MH * c + MH * u:4 * MH * c + MH * (u + 1)],
                                                xT[:, j % 2, c, :], start=c == 0, stop=c == 1)
                last.then_inc(s_gu, 1)

            def down(i, j):
                e = EB * i + j
                pe.wait_ge(s_h, e + 1)
                if due(e - 1):
                    pe.wait_ge(s_o, e - 1)
                for u in range(2):
                    last = nc.tensor.matmul(DP[j % 2][0:CAP, 0:E], hid[:, j % 2, u, :],
                                            wd[:, j, E * u:E * (u + 1)], start=u == 0, stop=u == 1)
                last.then_inc(s_d, 1)

            def back(i, j, k):
                return (i, j - k) if j >= k else (i - 1, j - k + EB)

            def body(i, more):
                for j in range(EB):
                    rows_t(i, j)
                    for part, k in ((gate_up, 1), (down, 2)):
                        if not (isinstance(i, int) and EB * i + j < k):
                            part(*back(i, j, k))

            steps(pe, body, n=NB)
            gate_up(NB - 1, EB - 1)
            down(NB - 1, EB - 2)
            down(NB - 1, EB - 1)

        @block.scalar
        def _(act):
            def save(i, j):
                e = EB * i + j
                act.wait_ge(s_x, e + 1)
                if due(e - 1):
                    act.wait_ge(s_gu, e - 1)
                nc.scalar.copy(xT[:, j % 2].rearrange("p c s -> p (c s)"), XP[j % 2][:, 0:2 * CAP]).then_inc(s_xe, 1)

            def silu(i, j):
                e = EB * i + j
                act.wait_ge(s_gu, e + 1)
                if due(e - 1):
                    act.wait_ge(s_h, e - 1)
                nc.scalar.activation(sil[:, j % 2], GP[j % 2][0:MH, 0:2 * CAP], ACT.Silu).then_inc(s_sil, 1)

            def body(i, more):
                for j in range(EB):
                    save(i, j)
                    if j >= 1:
                        silu(i, j - 1)
                    elif not first(i):
                        silu(i - 1, EB - 1)

            steps(act, body, n=NB)
            silu(NB - 1, EB - 1)

        @block.vector
        def _(dve):
            def lists(i):
                for j in range(EB):
                    if due(16 * i):
                        dve.wait_ge(s_g[j], 16 * i)
                nc.vector.tensor_copy(gidx[:], tokens[:, bass.ds(EB * i, EB)]).then_inc(s_gi, 1)

            def weights(i, j):
                e = EB * i + j
                dve.wait_ge(s_g[j], 16 * (i + 1))
                nc.vector.tensor_scalar(wcol[:, j:j + 1], xg[:, j, bass.ds(E + e, 1)], own[:], lastone[:],
                                        ALU.mult, ALU.add).then_inc(s_wc, 1)

            def hidden(i, j):
                e = EB * i + j
                dve.wait_ge(s_sil, e + 1)
                if due(e - 1):
                    dve.wait_ge(s_d, e - 1)
                nc.vector.tensor_tensor(hid[:, j % 2].rearrange("p u s -> p (u s)"), sil[:, j % 2],
                                        GP[j % 2][0:MH, 2 * CAP:4 * CAP], ALU.mult).then_inc(s_h, 1)

            def weigh(i, j):
                e = EB * i + j
                dve.wait_ge(s_d, e + 1)
                dve.wait_ge(s_wc, e + 1)
                if not first(i):
                    dve.wait_ge(s_s[j % 2], 16 * (EB // 2 * (i - 1) + j // 2 + 1))
                if due(16 * i):
                    dve.wait_ge(s_l[j], 16 * i)
                nc.vector.tensor_copy(sidx[:, j:j + 1], tokens[:, bass.ds(e, 1)]).then_inc(s_si, 1)
                nc.vector.tensor_scalar(outs[:, j, :], DP[j % 2][0:CAP, 0:E], wcol[:, j:j + 1], None,
                                        ALU.mult).then_inc(s_o, 1)

            lists(0)

            def body(i, more):
                for j in range(EB):
                    if j >= 1:
                        hidden(i, j - 1)
                    elif not first(i):
                        hidden(i - 1, EB - 1)
                    if j >= 2:
                        weigh(i, j - 2)
                    elif not first(i):
                        weigh(i - 1, j - 2 + EB)
                    weights(i, j)
                    if j == 2 and more:
                        lists(i + 1)

            steps(dve, body, apart=2, n=NB)
            hidden(NB - 1, EB - 1)
            weigh(NB - 1, EB - 2)
            weigh(NB - 1, EB - 1)

        @block.gpsimd
        def _(pool):
            def gather(i, j):
                e = EB * i + j
                if not first(i):
                    used, listed = ready(pool, EB * (i - 1) + j + 1), ready(pool, i + 1)
                    pool.wait_ge(s_x, 1)
                    pool.wait_ge(s_x, used)
                    pool.wait_ge(s_wc, used)
                    if j == 0:
                        pool.wait_ge(s_gi, listed)
                elif j == 0:
                    pool.wait_ge(s_gi, 1)
                pool.indirect_dma_start(xg[:, j, :], None, w["rows"],
                                        bass.IndirectOffsetOnAxis(ap=gidx[:, j:j + 1], axis=0)).then_inc(s_g[j], 16)

            def scatter(i, j):
                e = EB * i + j
                count, added = ready(pool, e + 1), ready(pool, 16 * (EB // 2 * i + j // 2))
                pool.wait_ge(s_o, 1)
                pool.wait_ge(s_o, count)
                pool.wait_ge(s_si, count)
                if due(added):
                    pool.wait_ge(s_s[j % 2], added)
                pool.indirect_dma_start(w["sums"][j % 2],
                                        bass.IndirectOffsetOnAxis(ap=sidx[0:CAP - 1, j:j + 1], axis=0),
                                        outs[0:CAP - 1, j, :], None, compute_op=ALU.add).then_inc(s_s[j % 2], 16)
                pool.dma_start(w["lasts"][bass.ds(e, 1), :], outs[CAP - 1:CAP, j, :]).then_inc(s_l[j], 16)

            for j in range(EB):
                gather(0, j)

            def body(i, more):
                for j in range(EB):
                    if j >= 3:
                        scatter(i, j - 3)
                    elif not first(i):
                        scatter(i - 1, j - 3 + EB)
                    if more:
                        gather(i + 1, j)

            steps(pool, body, n=NB)
            for j in range(EB - 3, EB):
                scatter(NB - 1, j)
            for j in range(EB):
                pool.wait_ge(s_s[j % 2], 16 * NE // 2)
                pool.wait_ge(s_l[j], 16 * NB)


def final_phase(nc, ctx, mem, w):
    def sem(name):
        return ctx.enter_context(nc.semaphore(f"f_{name}"))

    X, WK, lastsb, wov, y0, y1 = (mem[k] for k in ("X", "WK", "lastsb", "wov", "y0", "y1"))
    P = mem["banks"]
    s_last = sem("lasts")
    s_y = sem("sums_loaded")
    s_wv = sem("weights")
    s_ov = sem("over")
    s_sum = sem("sum")
    s_a = sem("added")
    s_x = sem("result")
    s_out = sem("stored")

    sums = [y[0:NT * 128, :].rearrange("(g t p) e -> g p t e", p=128, t=GT) for y in w["sums"]]
    out = w["out"].rearrange("(g t p) e -> g p t e", p=128, t=GT)
    with nc.Block() as block:
        @block.sync
        def _(sp):
            sp.dma_start(lastsb[:], w["lasts"]).then_inc(s_last, 16)

            def body(i, more):
                if due(i):
                    sp.wait_ge(s_a, i)
                if due(i):
                    sp.wait_ge(s_sum, i)
                sp.dma_start(y0[:], sums[0][i]).then_inc(s_y, 16)
                sp.dma_start(y1[:], sums[1][i]).then_inc(s_y, 16)

            steps(sp, body)

        @block.scalar
        def _(act):
            def body(i, more):
                if due(2 * i):
                    act.wait_ge(s_ov, 2 * i)
                nc.scalar.copy(wov[:], WK[0:NE, bass.ds(TOK * i, TOK)]).then_inc(s_wv, 1)
                act.wait_ge(s_x, 2 * (i + 1))
                act.dma_start(out[i], X[:, bass.ds(GT * i, GT), :]).then_inc(s_out, 16)

            steps(act, body)
            act.wait_ge(s_out, 16 * NG)

        @block.tensor
        def _(pe):
            pe.wait_ge(s_last, 16)

            def body(i, more):
                pe.wait_ge(s_wv, i + 1)
                for b in range(2):
                    if due(2 * i + b - 1):
                        pe.wait_ge(s_x, 2 * i + b - 1)
                    for t in range(2):
                        last = nc.tensor.matmul(P[b][:, E * t:E * (t + 1)], wov[:, 256 * b + 128 * t:256 * b + 128 * (t + 1)],
                                                lastsb[:], start=True, stop=True)
                    last.then_inc(s_ov, 1)

            steps(pe, body)

        @block.gpsimd
        def _(pool):
            def body(i, more):
                pool.wait_ge(s_y, 32 * (i + 1))
                nc.gpsimd.tensor_tensor(y0[:], y0[:], y1[:], ALU.add).then_inc(s_sum, 1)

            steps(pool, body)

        @block.vector
        def _(dve):
            def body(i, more):
                dve.wait_ge(s_sum, i + 1)
                xi = X[:, bass.ds(GT * i, GT), :]
                nc.vector.tensor_tensor(xi, xi, y0[:], ALU.add).then_inc(s_a, 1)
                dve.wait_ge(s_a, i + 1)
                for b in range(2):
                    dve.wait_ge(s_ov, 2 * i + b + 1)
                    xt = X[:, bass.ds(GT * i + 2 * b, 2), :]
                    nc.vector.tensor_tensor(xt, P[b][:].rearrange("p (t e) -> p t e", e=E), xt,
                                            ALU.add).then_inc(s_x, 1)

            steps(dve, body)


def decoder_layer(nc, x, ctx_rows, wq, bq, wk, bk, wv, bv, wc, bc, gate, sgu, sd, wgu, wd, out):
    ctx = ExitStack()
    with ctx:
        def sb(name, shape, dt=F32):
            return stack[-1].enter_context(nc.sbuf_tensor(name, shape, dt))

        def pb(name, shape, dt=F32):
            return stack[-1].enter_context(nc.psum_tensor(name, shape, dt))

        stack = [ctx]
        rows_d = nc.dram_tensor("rows_d", (NT * 128 + CAP, E + NE), F32, kind="Internal").ap()
        sums_d = [nc.dram_tensor(f"sum{k}_d", (NT * 128 + CAP, E), F32, kind="Internal").ap() for k in range(2)]
        lasts_d = nc.dram_tensor("lasts_d", (NE, E), F32, kind="Internal").ap()
        mem = {}
        mem["X"] = sb("X", [128, NT, E])
        mem["ident"] = sb("ident", [128, 128])
        mem["half_pow"] = sb("half_pow", [128, GT])
        mem["mv"] = sb("mv", [128, GT, 2])
        mem["st"] = sb("st", [128, GT, 6])
        mem["rstd"] = sb("rstd", [128, GT])
        w = dict(x=x, ctx=ctx_rows, wq=wq, bq=bq, wk=wk, bk=bk, wv=wv, bv=bv, wc=wc, bc=bc, rows=rows_d,
                 sums=sums_d, lasts=lasts_d, wgu=wgu, wd=wd, out=out)

        attn = ExitStack()
        stack.append(attn)
        zeros = sb("zeros", [128, (NT * 128 + CAP) * E // 512])
        mem["ident_bf"] = sb("ident_bf", [128, 128], BF16)
        mem["mask"] = sb("mask", [128, HH * S], BF16)
        mem["headmask"] = sb("headmask", [128, HH])
        mem["xh"] = sb("xh", [128, GT, E])
        mem["xhT"] = sb("xhT", [128, 2, TOK])
        mem["qT"] = sb("qT", [128, 2, TOK])
        mem["kT"] = sb("kT", [128, 2, TOK])
        mem["kbd"] = sb("kbd", [128, 2, GB, HH, S])
        mem["vT"] = sb("vT", [64, GB, 2, S])
        mem["vbd"] = sb("vbd", [128, GB, G, 2, VW])
        mem["ET"] = sb("ET", [128, 2, H // 2, 128])
        mem["E"] = sb("E", [128, 2, H * S])
        mem["mx"] = sb("mx", [128, 2, H])
        mem["rc"] = sb("rc", [128, 2, H])
        mem["att"] = sb("att", [128, 2, E])
        w["wq_sb"] = sb("wq_sb", [128, 2, E])
        w["wk_sb"] = sb("wk_sb", [128, 2, G * D])
        w["wv_sb"] = sb("wv_sb", [128, 2, G * D])
        w["wc_sb"] = sb("wc_sb", [128, 2, E])
        w["bq_sb"] = sb("bq_sb", [128, 2])
        w["bqs_sb"] = sb("bqs_sb", [128, 2])
        w["bk_sb"] = sb("bk_sb", [128, 2])
        w["bv_sb"] = sb("bv_sb", [64, 1])
        w["bc_sb"] = sb("bc_sb", [128, E])
        w["wkr_sb"] = sb("wkr_sb", [128, 2, E])
        w["ctxR"] = sb("ctxR", [128, GT, E])
        w["ctxA"] = sb("ctxA", [128, GT, G * D])
        w["ctx2"] = sb("ctx2", [128, GB, G * D])
        w["oT"] = sb("oT", [128, 2, 2, 128])

        mem["ring"] = [pb(f"ring{k}", [128, 512]) for k in range(NR)]
        mem["Sc"] = [pb(f"Sc{k}", [128, 2, 512]) for k in range(2)]
        mem["O"] = pb("O", [128, 512])

        s_const = ctx.enter_context(nc.semaphore("constants"))
        s_zero = ctx.enter_context(nc.semaphore("const_fill"))
        s_vconst = ctx.enter_context(nc.semaphore("constants_dve"))
        s_vzero = ctx.enter_context(nc.semaphore("values_fill"))
        s_ztile = ctx.enter_context(nc.semaphore("zero_tile"))
        s_zd = ctx.enter_context(nc.semaphore("dram_zeroed"))
        s_half = ctx.enter_context(nc.semaphore("const_half"))

        with nc.Block() as block:
            @block.gpsimd
            def _(pool):
                for n, (m, value) in enumerate(((mem["ident"], 0.0), (mem["mask"], 0.0))):
                    nc.gpsimd.memset(m[:], value).then_inc(s_zero, 1)
                pool.wait_ge(s_zero, 2)
                nc.gpsimd.affine_select(out=mem["ident"][:], in_=mem["ident"][:], compare_op=ALU.not_equal, fill=1.0,
                                        base=0, pattern=[[-1, 128]], channel_multiplier=1).then_inc(s_const, 1)
                for h in range(2):
                    m = mem["mask"][64 * h:64 * (h + 1), :].rearrange("p (h k) -> p h k", k=S)
                    pool.wait_ge(s_const, h + 1)
                    nc.gpsimd.affine_select(out=m, in_=m, compare_op=ALU.is_ge, fill=MASKED,
                                            base=0, pattern=[[0, HH], [-1, S]],
                                            channel_multiplier=1).then_inc(s_const, 1)
                pool.wait_ge(s_const, 3)
                nc.gpsimd.memset(mem["half_pow"][:], -0.5).then_inc(s_const, 1)

            @block.vector
            def _(dve):
                nc.vector.memset(zeros[:], 0.0).then_inc(s_ztile, 1)
                nc.vector.memset(mem["kbd"][:], 0.0)
                nc.vector.memset(mem["vbd"][:], 0.0).then_inc(s_vzero, 1)
                dve.wait_ge(s_vzero, 1)
                for h in range(2):
                    last = nc.vector.memset(mem["vbd"][64 * h:64 * (h + 1), :, :, h, D:VW], 1.0)
                last.then_inc(s_vconst, 1)
                dve.wait_ge(s_const, 1)
                nc.vector.tensor_copy(mem["ident_bf"][:], mem["ident"][:]).then_inc(s_vconst, 1)

            @block.scalar
            def _(act):
                act.wait_ge(s_ztile, 1)
                for y in sums_d:
                    for q in range(4):
                        act.dma_start(y.rearrange("r e -> (r e)").rearrange("(q p a) -> q p a", q=4, p=128)[q],
                                      zeros[:]).then_inc(s_zd, 16)
                act.dma_start(rows_d[NT * 128:, :], zeros[0:CAP, 0:E + NE]).then_inc(s_zd, 16)
                act.wait_ge(s_zd, 9 * 16)

        attention_phase(nc, ctx, mem, w, cross=False)
        attention_phase(nc, ctx, mem, w, cross=True)
        attn.close()
        stack.pop()

        mem["banks"] = [pb(f"bank{k}", [128, 512]) for k in range(8)]
        mem["WK"] = sb("WK", [128, NT * 128])
        mem["tokens"] = sb("tokens", [CAP, NE], I32)
        w["sgu_sb"] = sb("sgu_sb", [128, 2, 2 * MS])
        w["sd_sb"] = sb("sd_sb", [128, 3, E])
        w["wgu_sb"] = sb("wgu_sb", [128, EB, 8 * MH])
        w["wd_sb"] = sb("wd_sb", [MH, EB, 2 * E])
        w["s_w"] = [ctx.enter_context(nc.semaphore(f"expert_weights{j}")) for j in range(EB)]

        early = ExitStack()
        stack.append(early)
        mem["xnT"] = sb("xnT", [128, 2, NT * 128])
        mid = ExitStack()
        stack.append(mid)
        mem["gate"] = sb("gate_sb", [128, 2, NE])
        mem["desc"] = sb("desc", [128, NT * 128])
        mem["iota"] = sb("iota", [128, NE])
        mem["xn"] = sb("xn", [128, GT, E])
        mem["logT"] = sb("logT", [NE, TOK])
        mem["lg"] = sb("lg", [128, GT, NE])
        mem["m4"] = sb("m4", [128, GT])
        mem["r4"] = sb("r4", [128, GT])
        mem["sc"] = sb("sc", [128, GT, NE])
        mem["gs"] = sb("gs", [128, GT * NGRP])
        mem["g8"] = sb("g8", [128, GT, 8])
        mem["gi"] = sb("gi", [128, GT, 8], U32)
        mem["eqg"] = sb("eqg", [128, GT, NGRP, TOPG])
        mem["gm"] = sb("gm", [128, GT * NGRP])
        mem["tmp"] = sb("tmp", [128, GT, NE])
        mem["t8"] = sb("t8", [128, GT, 8])
        mem["ti"] = sb("ti", [128, GT, 8], U32)
        mem["eqe"] = sb("eqe", [128, 2, NE, TOPK])
        mem["wa"] = sb("wa", [128, GT, 2 * NE])

        s_gate = ctx.enter_context(nc.semaphore("router_inputs"))
        s_iota = ctx.enter_context(nc.semaphore("router_constants"))
        w["s_moe_in"] = ctx.enter_context(nc.semaphore("shared_weights"))
        w["n_moe_in"] = 48
        with nc.Block() as block:
            @block.sync
            def _(sp):
                sp.dma_start(mem["gate"][:], gate.rearrange("(c p) n -> p c n", p=128)).then_inc(s_gate, 16)
                sp.dma_start(w["sgu_sb"][:], sgu.rearrange("(c p) n -> p c n", p=128)).then_inc(w["s_moe_in"], 16)
                sp.dma_start(w["sd_sb"][:, 0:2, :], sd[0:256].rearrange("(c p) n -> p c n", p=128)).then_inc(w["s_moe_in"], 16)
                sp.dma_start(w["sd_sb"][0:MS - 256, 2, :], sd[256:MS]).then_inc(w["s_moe_in"], 16)
                for j in range(EB):
                    sp.dma_start(w["wgu_sb"][:, j, :], wgu[j]).then_inc(w["s_w"][j], 16)
                    sp.dma_start(w["wd_sb"][:, j, :], wd[j]).then_inc(w["s_w"][j], 16)
                sp.wait_ge(s_gate, 16)

            @block.gpsimd
            def _(pool):
                nc.gpsimd.iota(mem["iota"][:], pattern=[[1, NE]], base=0, channel_multiplier=0,
                               allow_small_or_imprecise_dtypes=True).then_inc(s_iota, 1)
                nc.gpsimd.iota(mem["desc"][:], pattern=[[-1, NT * 128]], base=NT * 128, channel_multiplier=0,
                               allow_small_or_imprecise_dtypes=True).then_inc(s_iota, 1)

        routing_phase(nc, ctx, mem, w)
        stack.pop()
        mid.close()
        sh = ExitStack()
        stack.append(sh)
        mem["kw"] = sb("kw", [128, NT * 128])
        mem["top"] = sb("top", [128, CAP])
        mem["tokf"] = sb("tokf", [128, CAP])
        mem["slot"] = sb("slot", [128, CAP])
        mem["mark"] = sb("mark", [128, CAP])
        mem["lastk"] = sb("lastk", [128, 3])
        mem["sg"] = sb("sg", [128, 3, TOK])
        mem["su"] = sb("su", [128, 3, TOK])
        mem["hT"] = sb("hT", [128, 3, TOK])
        mem["sh"] = sb("sh", [128, GT, E])
        with nc.Block() as block:
            @block.gpsimd
            def _(pool):
                nc.gpsimd.iota(mem["slot"][:], pattern=[[1, CAP]], base=0, channel_multiplier=0,
                               allow_small_or_imprecise_dtypes=True).then_inc(s_iota, 1)
        shared_phase(nc, ctx, mem, w)
        stack.pop()
        sh.close()
        stack.pop()
        early.close()

        mem["gidx"] = sb("gidx", [CAP, EB], I32)
        mem["sidx"] = sb("sidx", [CAP, EB], I32)
        mem["xg"] = sb("xg", [CAP, EB, E + NE])
        mem["xT"] = sb("xT", [128, 2, 2, CAP])
        mem["sil"] = sb("sil", [MH, 2, 2 * CAP])
        mem["hid"] = sb("hid", [MH, 2, 2, CAP])
        mem["outs"] = sb("outs", [CAP, EB, E])
        mem["wcol"] = sb("wcol", [CAP, EB])
        mem["own"] = sb("own", [CAP, 1])
        mem["lastone"] = sb("lastone", [CAP, 1])
        with nc.Block() as block:
            @block.gpsimd
            def _(pool):
                nc.gpsimd.memset(mem["own"][:], 1.0).then_inc(s_half, 1)
                nc.gpsimd.memset(mem["lastone"][:], 0.0).then_inc(s_half, 1)
                pool.wait_ge(s_half, 2)
                for m, op, fill in ((mem["own"], ALU.not_equal, 0.0), (mem["lastone"], ALU.not_equal, 1.0)):
                    nc.gpsimd.affine_select(out=m[:], in_=m[:], compare_op=op, fill=fill, base=-(CAP - 1),
                                            pattern=[[0, 1]], channel_multiplier=1).then_inc(s_half, 1)
        experts_phase(nc, ctx, mem, w)

        mem["lastsb"] = sb("lastsb", [NE, E])
        mem["wov"] = sb("wov", [NE, TOK])
        mem["y0"] = sb("y0", [128, GT, E])
        mem["y1"] = sb("y1", [128, GT, E])
        final_phase(nc, ctx, mem, w)


def kernel(**inputs):
    import numpy as np
    import concourse.bacc as bacc
    from concourse.bass_utils import run_bass_kernel_spmd

    a = {k.replace("L0_", ""): np.asarray(v) for k, v in inputs.items()}

    def rows_first(x):
        return x.transpose(1, 0, 2).reshape(E, -1)

    up = np.concatenate([a["ffn_Wg"], a["ffn_Wu"]], axis=1)
    arrays = {
        "x": a["x"].reshape(B * S, E),
        "ctx_rows": a["ctx_512"].reshape(B * S, G * D),
        "wq": rows_first(a["attn_Wq"]),
        "bq": a["attn_bq"].reshape(2, 128).T,
        "wk": rows_first(a["attn_Wk"]),
        "bk": a["attn_bk"].reshape(G * D, 1),
        "wv": rows_first(a["attn_Wv"]),
        "bv": a["attn_bv"].reshape(G * D, 1),
        "wc": a["xattn_Wc"].T,
        "bc": a["xattn_bc"],
        "gate": a["ffn_gate_weight"].T,
        "sgu": np.concatenate([a["ffn_Sg"], a["ffn_Su"]], axis=0).T,
        "sd": a["ffn_Sd"].T,
        "wgu": up.transpose(0, 2, 1).reshape(NE, 2, 128, 2 * M).transpose(0, 2, 1, 3).reshape(NE, 128, 4 * M),
        "wd": a["ffn_Wd"].transpose(0, 2, 1).reshape(NE, 2, MH, E).transpose(0, 2, 1, 3).reshape(NE, MH, 2 * E),
    }
    nc = bacc.Bacc("TRN2", target_bir_lowering=False, num_devices=1)
    ins, aps = {}, {}
    for name, x in arrays.items():
        ins[f"in_{name}_dram"] = np.ascontiguousarray(x)
        aps[name] = nc.dram_tensor(f"in_{name}_dram", x.shape, mybir.dt.from_np(x.dtype), kind="ExternalInput").ap()
    aps["out"] = nc.dram_tensor("out_dram", (B * S, E), F32, kind="ExternalOutput").ap()
    decoder_layer(nc, **aps)
    r = run_bass_kernel_spmd(nc, [ins], core_ids=[0])
    return r.results[0]["out_dram"].reshape(B, S, E)
```
